# Optimizing a Trainium2 kernel written in Bass

```python
import numpy as np
import jax
import jax.numpy as jnp

def _softmax(x, axis=-1):
    return jax.nn.softmax(x, axis=axis)

def _gelu(x):
    return jax.nn.gelu(x, approximate=True)

def _silu(x):
    return jax.nn.silu(x)

def _sigmoid(x):
    return jax.nn.sigmoid(x)

def _layernorm(x, axis=-1, eps=1e-05):
    m = jnp.mean(x, axis=axis, keepdims=True)
    v = jnp.var(x, axis=axis, keepdims=True)
    return (x - m) / jnp.sqrt(v + eps)

def _scatter_add(tgt, idx, src, axis=0):
    return tgt.at[idx].add(src)

def _segment_sum(src, seg, n):
    return jax.ops.segment_sum(src, seg, n)
kernel_name = 'mk_rec_standalone_d1_rec_r8_57d027'

def setup_inputs(seed: int=0):
    np.random.seed(seed)
    _w = jnp.asarray

    def _rec_inputs():
        import jax
        import jax.numpy as jnp
        _rk = jax.random.key(seed)
        r_interactions = jnp.stack([jax.random.randint(jax.random.fold_in(jax.random.fold_in(_rk, 1), 0), (512,), 1, 9997, jnp.int32), jax.random.randint(jax.random.fold_in(jax.random.fold_in(_rk, 1), 1), (512,), 7, 1250, jnp.int32)], axis=1)
        return r_interactions
    r_interactions = _rec_inputs()

    def _L0_rec_setup():
        import jax, jax.numpy as jnp
        import numpy as np
        NUM_USERS = 12500
        NUM_ITEMS = 1250
        USER_DIM = 32
        ITEM_DIM = 32
        H1 = 128
        H2 = 128
        BATCH = 512
        key = jax.random.key(seed)
        ks = jax.random.split(key, 10)
        interactions = jax.random.randint(ks[0], (BATCH, 2), 0, NUM_ITEMS, dtype=jnp.int64)
        users_emb_w = jax.random.normal(ks[1], (NUM_USERS, USER_DIM), dtype=jnp.float32)
        items_emb_w = jax.random.normal(ks[2], (NUM_ITEMS, ITEM_DIM), dtype=jnp.float32)
        d_in = USER_DIM + ITEM_DIM
        w1 = jax.random.normal(ks[3], (H1, d_in), dtype=jnp.float32) / np.sqrt(d_in)
        b1 = jnp.zeros((H1,), dtype=jnp.float32)
        w2 = jax.random.normal(ks[4], (H2, H1), dtype=jnp.float32) / np.sqrt(H1)
        b2 = jnp.zeros((H2,), dtype=jnp.float32)
        head_in = NUM_ITEMS + H2
        w_head = jax.random.normal(ks[5], (NUM_ITEMS, head_in), dtype=jnp.float32) / np.sqrt(head_in)
        b_head = jnp.zeros((NUM_ITEMS,), dtype=jnp.float32)
        return {'interactions': interactions, 'users_emb_w': users_emb_w, 'items_emb_w': items_emb_w, 'w1': w1, 'b1': b1, 'w2': w2, 'b2': b2, 'w_head': w_head, 'b_head': b_head}
    _L0_rec_all = _L0_rec_setup()
    _L0_rec_in = {k: v for k, v in _L0_rec_all.items() if k in ('users_emb_w', 'items_emb_w', 'w1', 'b1', 'w2', 'b2', 'w_head', 'b_head')}
    del _L0_rec_all
    return {'r_interactions': r_interactions, 'L0_rec_users_emb_w': _L0_rec_in['users_emb_w'], 'L0_rec_items_emb_w': _L0_rec_in['items_emb_w'], 'L0_rec_w1': _L0_rec_in['w1'], 'L0_rec_b1': _L0_rec_in['b1'], 'L0_rec_w2': _L0_rec_in['w2'], 'L0_rec_b2': _L0_rec_in['b2'], 'L0_rec_w_head': _L0_rec_in['w_head'], 'L0_rec_b_head': _L0_rec_in['b_head']}

def reference(r_interactions, L0_rec_users_emb_w, L0_rec_items_emb_w, L0_rec_w1, L0_rec_b1, L0_rec_w2, L0_rec_b2, L0_rec_w_head, L0_rec_b_head):
    import jax
    import jax.numpy as jnp

    def _L0_rec_ref(interactions, users_emb_w, items_emb_w, w1, b1, w2, b2, w_head, b_head):
        import jax, jax.numpy as jnp
        import numpy as np
        NUM_USERS = 12500
        NUM_ITEMS = 1250
        USER_DIM = 32
        ITEM_DIM = 32
        H1 = 128
        H2 = 128
        BATCH = 512
        users = interactions[:, 0]
        items = interactions[:, 1]
        all_embed = jnp.concatenate([users_emb_w[users], items_emb_w[items]], axis=1)
        h = jax.nn.relu(all_embed @ w1.T + b1)
        h = jax.nn.relu(h @ w2.T + b2)
        cross = jax.nn.one_hot(items, NUM_ITEMS, dtype=h.dtype)
        head_in = jnp.concatenate([cross, h], axis=1)
        return jax.nn.sigmoid(head_in @ w_head.T + b_head)
    y = _L0_rec_ref(r_interactions, L0_rec_users_emb_w, L0_rec_items_emb_w, L0_rec_w1, L0_rec_b1, L0_rec_w2, L0_rec_b2, L0_rec_w_head, L0_rec_b_head)
    return y

_drawn_inputs = setup_inputs


def setup_inputs(seed=0):
    import zlib

    import numpy as np

    out = dict(_drawn_inputs(seed))
    spreads = {'L0_rec_b1': (0.0, 0.8), 'L0_rec_b2': (0.0, 0.762), 'L0_rec_b_head': (0.0, 0.1)}
    factors = {}
    for name, (base, spread) in spreads.items():
        noise = np.random.default_rng([zlib.crc32(name.encode()), seed]).standard_normal(out[name].shape)
        drawn = base * np.exp(spread * noise) if base else spread * noise
        out[name] = jnp.asarray(drawn.astype(out[name].dtype))
    for name, factor in factors.items():
        out[name] = (out[name] * factor).astype(out[name].dtype)
    return out
```

```python
from contextlib import ExitStack

import concourse.bass as bass
from concourse import mybir

ALU = mybir.AluOpType
ACT = mybir.ActivationFunctionType
F32 = mybir.dt.float32
BF16 = mybir.dt.bfloat16
I32 = mybir.dt.int32

P = 128
BANK = 512
DMA = 16
BIAS_PARTS = 3


def rec_scores_kernel(nc: bass.Bass, interactions: bass.AP, users_emb: bass.AP, item_rows: bass.AP,
                      mlp_weights: bass.AP, head_h: bass.AP, b_head: bass.AP, out: bass.AP):
    B = interactions.shape[0]
    T = B // P
    DU = users_emb.shape[1]
    N = head_h.shape[1]
    DI = item_rows.shape[1] - N
    D = DU + DI
    H = head_h.shape[0]
    BP = b_head.shape[0]
    BC = b_head.shape[1]
    NB = -(-N // BANK)
    W = -(-N // NB)
    W += W % 2
    cols = [(c * W, min(N, (c + 1) * W)) for c in range(NB)]
    assert B % P == 0 and H == P and BP * BC == N

    with ExitStack() as ctx:
        def sb(name, shape, dt=F32):
            return ctx.enter_context(nc.sbuf_tensor(name, shape, dt))

        def psum(name, shape):
            return ctx.enter_context(nc.psum_tensor(name, shape, F32))

        def sem(name):
            return ctx.enter_context(nc.semaphore(name))

        index = sb("index", [P, T, 2], I32)
        rows = sb("rows", [P, T, D + N])
        probs = sb("probs", [P, T, N])
        mlp_w = sb("mlp_w", [P, 2 * H + 2])
        w1T = mlp_w[0:D, 0:H]
        w2T = mlp_w[:, H:2 * H]
        b1 = mlp_w[:, 2 * H:2 * H + 1]
        b2 = mlp_w[:, 2 * H + 1:2 * H + 2]
        head_w = sb("head_w", [H, N])
        bias_raw = sb("bias_raw", [BP, BC])
        bias_rest = sb("bias_rest", [BP, 2, BC])
        bias_part = sb("bias_part", [BP, BIAS_PARTS, BC], BF16)
        bias_rows = sb("bias_rows", [BIAS_PARTS, N], BF16)
        ones = sb("ones", [BIAS_PARTS, P], BF16)
        ident = sb("ident", [P, P])
        warm = sb("warm", [P, 1])
        embT = sb("embT", [D, 2, P])
        h1 = sb("h1", [H, 2, P])
        h2 = sb("h2", [H, 2, P])
        mlp_ps = psum("mlp_ps", [P, 2, BANK])
        score_ps = psum("score_ps", [P, 2 * NB, BANK])

        index_in = sem("index_in")
        weights_in = sem("weights_in")
        head_in = sem("head_in")
        bias_in = sem("bias_in")
        bias_rows_in = [sem(f"bias_rows_in{k}") for k in range(BIAS_PARTS)]
        users_in = [sem(f"users_in{t}") for t in range(T)]
        items_in = [sem(f"items_in{t}") for t in range(T)]
        ident_step = sem("ident_step")
        ones_set = sem("ones_set")
        bias_step = sem("bias_step")
        turned = sem("turned")
        embT_set = sem("embT_set")
        layer1 = sem("layer1")
        h1_set = sem("h1_set")
        layer2 = sem("layer2")
        h2_set = sem("h2_set")
        scored = sem("scored")
        added = sem("added")
        probs_set = sem("probs_set")
        stored = sem("stored")

        out_rows = out.rearrange("(p t) n -> p t n", t=T)
        block = ctx.enter_context(nc.Block())

        @block.sync
        def _(sp):
            sp.dma_start(index[:, :, :], interactions.rearrange("(p t) k -> p t k", t=T)).then_inc(index_in, DMA)
            sp.dma_start(bias_raw[:, :], b_head).then_inc(bias_in, DMA)
            sp.dma_start(mlp_w[:, :], mlp_weights).then_inc(weights_in, DMA)
            for k in range(BIAS_PARTS):
                sp.wait_ge(bias_step, 1 + 2 * k)
                sp.dma_start(bias_rows[k:k + 1, :], bias_part[:, k, :]).then_inc(bias_rows_in[k], DMA)
            for t in range(T):
                for c, (a, b) in enumerate(cols):
                    sp.wait_ge(probs_set, NB * t + c + 1)
                    sp.dma_start(out_rows[:, t, a:b], probs[:, t, a:b]).then_inc(stored, DMA)
            sp.wait_ge(stored, DMA * T * NB)

        @block.gpsimd
        def _(pool):
            pool.memset(ident[:, :], 0.0).then_inc(ident_step, 1)
            pool.wait_ge(ident_step, 1)
            pool.affine_select(out=ident[:, :], in_=ident[:, :], compare_op=ALU.not_equal, fill=1.0,
                               base=0, pattern=[[-1, P]], channel_multiplier=1).then_inc(ident_step, 1)
            pool.wait_ge(index_in, DMA)
            for t in range(T):
                pool.indirect_dma_start(
                    out=rows[:, t, 0:DU], out_offset=None, in_=users_emb,
                    in_offset=bass.IndirectOffsetOnAxis(ap=index[:, t, 0:1], axis=0)).then_inc(users_in[t], DMA)
                pool.indirect_dma_start(
                    out=rows[:, t, DU:D + N], out_offset=None, in_=item_rows,
                    in_offset=bass.IndirectOffsetOnAxis(ap=index[:, t, 1:2], axis=0)).then_inc(items_in[t], DMA)

        @block.tensor
        def _(pe):
            def turn(t):
                pe.wait_ge(users_in[t], DMA)
                pe.wait_ge(items_in[t], DMA)
                pe.transpose(mlp_ps[0:D, t % 2, 0:P], rows[:, t, 0:D], ident[:, :]).then_inc(turned, 1)

            def first(t):
                pe.wait_ge(embT_set, t + 1)
                pe.matmul(mlp_ps[:, t % 2, 0:P], w1T, embT[:, t % 2, :], start=True, stop=True).then_inc(layer1, 1)

            def second(t):
                pe.wait_ge(h1_set, t + 1)
                pe.matmul(mlp_ps[:, t % 2, 0:P], w2T, h1[:, t % 2, :], start=True, stop=True).then_inc(layer2, 1)

            def score(t, c):
                a, b = cols[c]
                if c == 0:
                    pe.wait_ge(h2_set, t + 1)
                if t >= 2:
                    pe.wait_ge(added, NB * (t - 2) + c + 1)
                bank = score_ps[:, NB * (t % 2) + c, 0:b - a]
                pe.matmul(bank, h2[:, t % 2, :], head_w[:, a:b], start=True, stop=False)
                pe.matmul(bank, ones[:, :], bias_rows[:, a:b], start=False, stop=True).then_inc(scored, 1)

            pe.wait_ge(ident_step, 2)
            pe.wait_ge(weights_in, DMA)
            turn(0)
            first(0)
            second(0)
            pe.wait_ge(head_in, DMA)
            pe.wait_ge(ones_set, 1)
            for k in range(BIAS_PARTS):
                pe.wait_ge(bias_rows_in[k], DMA)
            for t in range(T):
                score(t, 0)
                if t + 1 < T:
                    turn(t + 1)
                score(t, 1)
                if t + 1 < T:
                    first(t + 1)
                score(t, 2)
                if t + 1 < T:
                    second(t + 1)

        @block.vector
        def _(dve):
            dve.memset(ones[:, :], 1.0).then_inc(ones_set, 1)
            dve.wait_ge(bias_in, DMA)
            rest = bias_raw[:, :]
            for k in range(BIAS_PARTS):
                dve.tensor_copy(bias_part[:, k, :], rest).then_inc(bias_step, 1)
                if k < BIAS_PARTS - 1:
                    dve.wait_ge(bias_step, 2 * k + 1)
                    dve.tensor_tensor(bias_rest[:, k, :], rest, bias_part[:, k, :], ALU.subtract).then_inc(bias_step, 1)
                    dve.wait_ge(bias_step, 2 * k + 2)
                    rest = bias_rest[:, k, :]

            def relu1(t):
                dve.wait_ge(layer1, t + 1)
                dve.tensor_scalar(h1[:, t % 2, :], mlp_ps[:, t % 2, 0:P], b1, 0.0, ALU.add, ALU.max).then_inc(h1_set, 1)

            def add(t, c):
                a, b = cols[c]
                dve.wait_ge(scored, NB * t + c + 1)
                dve.tensor_tensor(rows[:, t, D + a:D + b], score_ps[:, NB * (t % 2) + c, 0:b - a],
                                  rows[:, t, D + a:D + b], ALU.add).then_inc(added, 1)

            dve.wait_ge(weights_in, DMA)
            relu1(0)
            for t in range(T):
                dve.wait_ge(items_in[t], DMA)
                add(t, 0)
                add(t, 1)
                if t + 1 < T:
                    relu1(t + 1)
                add(t, 2)

        @block.scalar
        def _(act):
            act.dma_start(head_w[:, :], head_h).then_inc(head_in, DMA)
            act.wait_ge(ident_step, 2)
            act.activation(warm[:, :], ident[:, 0:1], ACT.Sigmoid)

            def copy_embT(t):
                act.wait_ge(turned, t + 1)
                act.activation(embT[:, t % 2, :], mlp_ps[0:D, t % 2, 0:P], ACT.Copy).then_inc(embT_set, 1)

            def relu2(t):
                act.wait_ge(layer2, t + 1)
                act.activation(h2[:, t % 2, :], mlp_ps[:, t % 2, 0:P], ACT.Relu, bias=b2).then_inc(h2_set, 1)

            def sigmoid(t, c):
                a, b = cols[c]
                act.wait_ge(added, NB * t + c + 1)
                act.activation(probs[:, t, a:b], rows[:, t, D + a:D + b], ACT.Sigmoid).then_inc(probs_set, 1)

            act.wait_ge(weights_in, DMA)
            copy_embT(0)
            relu2(0)
            for t in range(T):
                sigmoid(t, 0)
                if t + 1 < T:
                    copy_embT(t + 1)
                sigmoid(t, 1)
                sigmoid(t, 2)
                if t + 1 < T:
                    relu2(t + 1)


def kernel(r_interactions, L0_rec_users_emb_w, L0_rec_items_emb_w, L0_rec_w1, L0_rec_b1, L0_rec_w2, L0_rec_b2,
           L0_rec_w_head, L0_rec_b_head):
    import numpy as np
    import concourse.bacc as bacc
    from concourse.bass_utils import run_bass_kernel_spmd

    n_items = L0_rec_items_emb_w.shape[0]
    hidden, d_in = L0_rec_w1.shape
    headT = np.ascontiguousarray(np.transpose(L0_rec_w_head))
    item_rows = np.concatenate([L0_rec_items_emb_w, headT[0:n_items]], axis=1)
    mlp_weights = np.zeros((hidden, 2 * hidden + 2), dtype=L0_rec_w1.dtype)
    mlp_weights[0:d_in, 0:hidden] = np.transpose(L0_rec_w1)
    mlp_weights[:, hidden:2 * hidden] = np.transpose(L0_rec_w2)
    mlp_weights[:, 2 * hidden] = L0_rec_b1
    mlp_weights[:, 2 * hidden + 1] = L0_rec_b2
    spread = max(p for p in range(1, 129) if n_items % p == 0)
    arrays = {
        "interactions": np.ascontiguousarray(r_interactions),
        "users_emb": np.ascontiguousarray(L0_rec_users_emb_w),
        "item_rows": np.ascontiguousarray(item_rows),
        "mlp_weights": mlp_weights,
        "head_h": np.ascontiguousarray(headT[n_items:]),
        "b_head": np.ascontiguousarray(np.reshape(L0_rec_b_head, (spread, n_items // spread))),
    }
    nc = bacc.Bacc("TRN2", target_bir_lowering=False, num_devices=1)
    args = [nc.dram_tensor(name, a.shape, mybir.dt.from_np(a.dtype), kind="ExternalInput").ap()
            for name, a in arrays.items()]
    out = nc.dram_tensor("scores", (r_interactions.shape[0], n_items), F32, kind="ExternalOutput").ap()
    rec_scores_kernel(nc, *args, out)
    ran = run_bass_kernel_spmd(nc, [arrays], core_ids=[0])
    return ran.results[0]["scores"]
```

```python
from contextlib import ExitStack

import concourse.bass as bass
from concourse import mybir

ALU = mybir.AluOpType
ACT = mybir.ActivationFunctionType
F32 = mybir.dt.float32
BF16 = mybir.dt.bfloat16
I32 = mybir.dt.int32

P = 128
BANK = 512
WITH_ROW = 1
WARM_UPS = 12
DMA = 16
BIAS_PARTS = 3


def rec_scores_kernel(nc: bass.Bass, interactions: bass.AP, users_emb: bass.AP, items_emb: bass.AP, item_rows: bass.AP,
                      mlp_weights: bass.AP, head_h: bass.AP, b_head: bass.AP, out: bass.AP):
    B = interactions.shape[0]
    T = B // P
    DU = users_emb.shape[1]
    N = head_h.shape[1]
    DI = items_emb.shape[1]
    D = DU + DI
    H = head_h.shape[0]
    BP = b_head.shape[0]
    BC = b_head.shape[1]
    NB = -(-N // BANK)
    cols = [(c * BANK, min(N, (c + 1) * BANK)) for c in range(NB)]
    assert B % P == 0 and H == P and BP * BC == N

    with ExitStack() as ctx:
        def sb(name, shape, dt=F32):
            return ctx.enter_context(nc.sbuf_tensor(name, shape, dt))

        def psum(name, shape):
            return ctx.enter_context(nc.psum_tensor(name, shape, F32))

        def sem(name):
            return ctx.enter_context(nc.semaphore(name))

        index = sb("index", [P, T, 2], I32)
        rows = sb("rows", [P, T, D + N])
        scores = rows[:, :, D:D + N]
        early_emb = sb("early_emb", [P, T, D])
        probs = sb("probs", [P, T, N])
        mlp_w = sb("mlp_w", [P, 2 * H + 2])
        w1T = mlp_w[0:D, 0:H]
        w2T = mlp_w[:, H:2 * H]
        b1 = mlp_w[:, 2 * H:2 * H + 1]
        b2 = mlp_w[:, 2 * H + 1:2 * H + 2]
        head_w = sb("head_w", [H, N])
        bias_raw = sb("bias_raw", [BP, BC])
        bias_rest = sb("bias_rest", [BP, 2, BC])
        bias_part = sb("bias_part", [BP, BIAS_PARTS, BC], BF16)
        bias_rows = sb("bias_rows", [BIAS_PARTS, N], BF16)
        ones = sb("ones", [BIAS_PARTS, P], BF16)
        ident = sb("ident", [P, P])
        warm = sb("warm", [P, 1])
        embT = sb("embT", [D, 2, P])
        h1 = sb("h1", [H, 2, P])
        h2 = sb("h2", [H, 2, P])
        mlp_ps = psum("mlp_ps", [P, 2, BANK])
        score_ps = psum("score_ps", [P, 2 * NB, BANK])

        emb = [rows[:, t, 0:D] if t == WITH_ROW else early_emb[:, t, :] for t in range(T)]

        index_in = sem("index_in")
        weights_in = sem("weights_in")
        head_in = sem("head_in")
        bias_in = sem("bias_in")
        bias_rows_in = [sem(f"bias_rows_in{k}") for k in range(BIAS_PARTS)]
        users_in = [sem(f"users_in{t}") for t in range(T)]
        items_in = [sem(f"items_in{t}") for t in range(T)]
        rows_in = [sem(f"rows_in{t}") for t in range(T)]
        items_in[WITH_ROW] = rows_in[WITH_ROW]
        ident_step = sem("ident_step")
        ones_set = sem("ones_set")
        bias_step = sem("bias_step")
        turned = sem("turned")
        embT_set = sem("embT_set")
        layer1 = sem("layer1")
        h1_set = sem("h1_set")
        layer2 = sem("layer2")
        h2_set = sem("h2_set")
        scored = sem("scored")
        added = sem("added")
        probs_set = sem("probs_set")
        stored = sem("stored")

        out_rows = out.rearrange("(p t) n -> p t n", t=T)
        block = ctx.enter_context(nc.Block())

        @block.sync
        def _(sp):
            sp.dma_start(index[:, :, :], interactions.rearrange("(p t) k -> p t k", t=T)).then_inc(index_in, DMA)
            sp.dma_start(mlp_w[:, :], mlp_weights).then_inc(weights_in, DMA)
            for k in range(BIAS_PARTS):
                sp.wait_ge(bias_step, 1 + 2 * k)
                sp.dma_start(bias_rows[k:k + 1, :], bias_part[:, k, :]).then_inc(bias_rows_in[k], DMA)
            for t in range(T):
                for c, (a, b) in enumerate(cols):
                    sp.wait_ge(probs_set, NB * t + c + 1)
                    sp.dma_start(out_rows[:, t, a:b], probs[:, t, a:b]).then_inc(stored, DMA)
            sp.wait_ge(stored, DMA * T * NB)

        @block.gpsimd
        def _(pool):
            pool.memset(ident[:, :], 0.0).then_inc(ident_step, 1)
            pool.wait_ge(ident_step, 1)
            pool.affine_select(out=ident[:, :], in_=ident[:, :], compare_op=ALU.not_equal, fill=1.0,
                               base=0, pattern=[[-1, P]], channel_multiplier=1).then_inc(ident_step, 1)
            pool.wait_ge(index_in, DMA)

            def gather(out, table, t, which, landed):
                pool.indirect_dma_start(
                    out=out, out_offset=None, in_=table,
                    in_offset=bass.IndirectOffsetOnAxis(ap=index[:, t, which:which + 1], axis=0)).then_inc(landed, DMA)

            def users(t):
                gather(emb[t][:, 0:DU], users_emb, t, 0, users_in[t])

            def items(t):
                gather(emb[t][:, DU:D], items_emb, t, 1, items_in[t])

            def whole_rows(t):
                gather(rows[:, t, DU:D + N], item_rows, t, 1, rows_in[t])

            users(0)
            items(0)
            whole_rows(1)
            users(1)
            whole_rows(0)
            for t in range(2, T):
                users(t)
                items(t)
                whole_rows(t)

        @block.tensor
        def _(pe):
            def turn(t):
                pe.wait_ge(users_in[t], DMA)
                pe.wait_ge(items_in[t], DMA)
                pe.transpose(mlp_ps[0:D, t % 2, 0:P], emb[t], ident[:, :]).then_inc(turned, 1)

            def first(t):
                pe.wait_ge(embT_set, t + 1)
                pe.matmul(mlp_ps[:, t % 2, 0:P], w1T, embT[:, t % 2, :], start=True, stop=True).then_inc(layer1, 1)

            def second(t):
                pe.wait_ge(h1_set, t + 1)
                pe.matmul(mlp_ps[:, t % 2, 0:P], w2T, h1[:, t % 2, :], start=True, stop=True).then_inc(layer2, 1)

            def bias(t, c):
                a, b = cols[c]
                if t >= 2:
                    pe.wait_ge(added, NB * (t - 2) + c + 1)
                pe.matmul(score_ps[:, NB * (t % 2) + c, 0:b - a], ones[:, :], bias_rows[:, a:b],
                          start=True, stop=False)

            def score(t, c):
                a, b = cols[c]
                if c == 0:
                    pe.wait_ge(h2_set, t + 1)
                pe.matmul(score_ps[:, NB * (t % 2) + c, 0:b - a], h2[:, t % 2, :], head_w[:, a:b],
                          start=False, stop=True).then_inc(scored, 1)

            def keep_warm(n):
                for _ in range(n):
                    pe.matmul(score_ps[:, 2 * NB - 1, 0:P], ident[:, :], ident[:, :], start=True, stop=True)

            pe.wait_ge(ident_step, 2)
            keep_warm(WARM_UPS)
            pe.wait_ge(weights_in, DMA)
            turn(0)
            keep_warm(1)
            pe.wait_ge(ones_set, 1)
            for k in range(BIAS_PARTS):
                pe.wait_ge(bias_rows_in[k], DMA)
            bias(0, 0)
            bias(0, 1)
            first(0)
            keep_warm(2)
            bias(0, 2)
            bias(1, 0)
            second(0)
            keep_warm(2)
            bias(1, 1)
            bias(1, 2)
            turn(1)
            pe.wait_ge(head_in, DMA)
            for t in range(T):
                if t >= 2:
                    bias(t, 0)
                score(t, 0)
                if t + 1 < T:
                    first(t + 1)
                if t >= 2:
                    bias(t, 1)
                score(t, 1)
                if t + 1 < T:
                    second(t + 1)
                if t >= 2:
                    bias(t, 2)
                score(t, 2)
                if t + 2 < T:
                    turn(t + 2)

        @block.vector
        def _(dve):
            dve.memset(ones[:, :], 1.0).then_inc(ones_set, 1)
            dve.wait_ge(bias_in, DMA)
            rest = bias_raw[:, :]
            for k in range(BIAS_PARTS):
                dve.tensor_copy(bias_part[:, k, :], rest).then_inc(bias_step, 1)
                if k < BIAS_PARTS - 1:
                    dve.wait_ge(bias_step, 2 * k + 1)
                    dve.tensor_tensor(bias_rest[:, k, :], rest, bias_part[:, k, :], ALU.subtract).then_inc(bias_step, 1)
                    dve.wait_ge(bias_step, 2 * k + 2)
                    rest = bias_rest[:, k, :]

            def relu1(t):
                dve.wait_ge(layer1, t + 1)
                dve.tensor_scalar(h1[:, t % 2, :], mlp_ps[:, t % 2, 0:P], b1, 0.0, ALU.add, ALU.max).then_inc(h1_set, 1)

            def add(t, c):
                a, b = cols[c]
                dve.wait_ge(scored, NB * t + c + 1)
                dve.tensor_tensor(scores[:, t, a:b], score_ps[:, NB * (t % 2) + c, 0:b - a],
                                  scores[:, t, a:b], ALU.add).then_inc(added, 1)

            dve.wait_ge(weights_in, DMA)
            relu1(0)
            for t in range(T):
                if t + 1 < T:
                    relu1(t + 1)
                dve.wait_ge(rows_in[t], DMA)
                for c in range(NB):
                    add(t, c)

        @block.scalar
        def _(act):
            act.dma_start(bias_raw[:, :], b_head).then_inc(bias_in, DMA)
            act.dma_start(head_w[:, :], head_h).then_inc(head_in, DMA)
            act.wait_ge(ident_step, 2)
            act.activation(warm[:, :], ident[:, 0:1], ACT.Sigmoid)

            def copy_embT(t):
                act.wait_ge(turned, t + 1)
                act.activation(embT[:, t % 2, :], mlp_ps[0:D, t % 2, 0:P], ACT.Copy).then_inc(embT_set, 1)

            def relu2(t):
                act.wait_ge(layer2, t + 1)
                act.activation(h2[:, t % 2, :], mlp_ps[:, t % 2, 0:P], ACT.Relu, bias=b2).then_inc(h2_set, 1)

            def sigmoid(t, c):
                a, b = cols[c]
                act.wait_ge(added, NB * t + c + 1)
                act.activation(probs[:, t, a:b], scores[:, t, a:b], ACT.Sigmoid).then_inc(probs_set, 1)

            act.wait_ge(weights_in, DMA)
            copy_embT(0)
            relu2(0)
            copy_embT(1)
            for t in range(T):
                if t + 1 < T:
                    relu2(t + 1)
                if t + 2 < T:
                    copy_embT(t + 2)
                for c in range(NB):
                    sigmoid(t, c)


def kernel(r_interactions, L0_rec_users_emb_w, L0_rec_items_emb_w, L0_rec_w1, L0_rec_b1, L0_rec_w2, L0_rec_b2,
           L0_rec_w_head, L0_rec_b_head):
    import numpy as np
    import concourse.bacc as bacc
    from concourse.bass_utils import run_bass_kernel_spmd

    n_items = L0_rec_items_emb_w.shape[0]
    hidden, d_in = L0_rec_w1.shape
    headT = np.ascontiguousarray(np.transpose(L0_rec_w_head))
    item_rows = np.concatenate([L0_rec_items_emb_w, headT[0:n_items]], axis=1)
    mlp_weights = np.zeros((hidden, 2 * hidden + 2), dtype=L0_rec_w1.dtype)
    mlp_weights[0:d_in, 0:hidden] = np.transpose(L0_rec_w1)
    mlp_weights[:, hidden:2 * hidden] = np.transpose(L0_rec_w2)
    mlp_weights[:, 2 * hidden] = L0_rec_b1
    mlp_weights[:, 2 * hidden + 1] = L0_rec_b2
    spread = max(p for p in range(1, 129) if n_items % p == 0)
    arrays = {
        "interactions": np.ascontiguousarray(r_interactions),
        "users_emb": np.ascontiguousarray(L0_rec_users_emb_w),
        "items_emb": np.ascontiguousarray(L0_rec_items_emb_w),
        "item_rows": np.ascontiguousarray(item_rows),
        "mlp_weights": mlp_weights,
        "head_h": np.ascontiguousarray(headT[n_items:]),
        "b_head": np.ascontiguousarray(np.reshape(L0_rec_b_head, (spread, n_items // spread))),
    }
    nc = bacc.Bacc("TRN2", target_bir_lowering=False, num_devices=1)
    args = [nc.dram_tensor(name, a.shape, mybir.dt.from_np(a.dtype), kind="ExternalInput").ap()
            for name, a in arrays.items()]
    out = nc.dram_tensor("item_probs", (r_interactions.shape[0], n_items), F32, kind="ExternalOutput").ap()
    rec_scores_kernel(nc, *args, out)
    ran = run_bass_kernel_spmd(nc, [arrays], core_ids=[0])
    return ran.results[0]["item_probs"]
```

```python
from contextlib import ExitStack

import concourse.bass as bass
from concourse import mybir

ALU = mybir.AluOpType
ACT = mybir.ActivationFunctionType
F32 = mybir.dt.float32
BF16 = mybir.dt.bfloat16
I32 = mybir.dt.int32

P = 128
BANK = 512
SCORE_BANKS = 7
WARM_UPS = 11
DMA = 16
BIAS_PARTS = 3


def rec_scores_kernel(nc: bass.Bass, interactions: bass.AP, users_emb: bass.AP, items_emb: bass.AP, item_rows: bass.AP,
                      mlp_weights: bass.AP, head_h: bass.AP, b_head: bass.AP, out: bass.AP):
    B = interactions.shape[0]
    T = B // P
    DU = users_emb.shape[1]
    N = head_h.shape[1]
    DI = items_emb.shape[1]
    D = DU + DI
    H = head_h.shape[0]
    BP = b_head.shape[0]
    BC = b_head.shape[1]
    NB = -(-N // BANK)
    even = [c * (-(-N // NB)) for c in range(NB)] + [N]
    falling = [N * part // 25 for part in (0, 7, 14, 20, 25)]
    whole = list(zip(even[:-1], even[1:]))
    cols = [whole] * (T - 1) + [list(zip(falling[:-1], falling[1:]))]
    start = [len(whole) * t for t in range(T)]
    chunks = start[-1] + len(cols[-1])
    assert B % (2 * P) == 0 and T > 3 and H == P and BP * BC == N and NB == 3

    with ExitStack() as ctx:
        def sb(name, shape, dt=F32):
            return ctx.enter_context(nc.sbuf_tensor(name, shape, dt))

        def psum(name, shape):
            return ctx.enter_context(nc.psum_tensor(name, shape, F32))

        def sem(name):
            return ctx.enter_context(nc.semaphore(name))

        index = sb("index", [P, T, 2], I32)
        rows = sb("rows", [P, T, D + N])
        scores = rows[:, :, D:D + N]
        early_emb = sb("early_emb", [P, T // 2, D])
        probs = sb("probs", [P, T, N])
        mlp_w = sb("mlp_w", [P, 2 * H + 2])
        w1T = mlp_w[0:D, 0:H]
        w2T = mlp_w[:, H:2 * H]
        b1 = mlp_w[:, 2 * H:2 * H + 1]
        b2 = mlp_w[:, 2 * H + 1:2 * H + 2]
        head_w = sb("head_w", [H, N])
        bias_raw = sb("bias_raw", [BP, BC])
        bias_rest = sb("bias_rest", [BP, 2, BC])
        bias_part = sb("bias_part", [BP, BIAS_PARTS, BC], BF16)
        bias_rows = sb("bias_rows", [BIAS_PARTS, N], BF16)
        bias_wide = sb("bias_wide", [P, N])
        ones = sb("ones", [BIAS_PARTS, P], BF16)
        ident = sb("ident", [P, P])
        warm = sb("warm", [P, 1])
        embT = sb("embT", [D, 2, P])
        h1 = sb("h1", [H, 2, P])
        h2 = sb("h2", [H, 2, P])
        mlp_ps = psum("mlp_ps", [P, BANK])
        score_ps = psum("score_ps", [P, SCORE_BANKS, BANK])

        emb = [early_emb[:, t // 2, :] if t % 2 == 0 else rows[:, t, 0:D] for t in range(T)]

        index_in = sem("index_in")
        weights_in = sem("weights_in")
        head_in = sem("head_in")
        bias_in = sem("bias_in")
        bias_rows_in = [sem(f"bias_rows_in{k}") for k in range(BIAS_PARTS)]
        users_in = [sem(f"users_in{t}") for t in range(T)]
        rows_in = [sem(f"rows_in{t}") for t in range(T)]
        items_in = [sem(f"items_in{t}") if t % 2 == 0 else rows_in[t] for t in range(T)]
        ident_step = sem("ident_step")
        ones_set = sem("ones_set")
        bias_step = sem("bias_step")
        bias_made = sem("bias_made")
        bias_copied = sem("bias_copied")
        biased = sem("biased")
        turned = sem("turned")
        embT_set = sem("embT_set")
        layer1 = sem("layer1")
        h1_set = sem("h1_set")
        layer2 = sem("layer2")
        h2_set = sem("h2_set")
        scored = sem("scored")
        added = sem("added")
        probs_set = sem("probs_set")
        stored = sem("stored")

        out_rows = out.rearrange("(p t) n -> p t n", t=T)
        block = ctx.enter_context(nc.Block())

        @block.sync
        def _(sp):
            sp.dma_start(index[:, :, :], interactions.rearrange("(p t) k -> p t k", t=T)).then_inc(index_in, DMA)
            sp.dma_start(mlp_w[:, :], mlp_weights).then_inc(weights_in, DMA)
            for k in range(BIAS_PARTS):
                sp.wait_ge(bias_step, 1 + 2 * k)
                sp.dma_start(bias_rows[k:k + 1, :], bias_part[:, k, :]).then_inc(bias_rows_in[k], DMA)
            for t in range(T):
                for c, (a, b) in enumerate(cols[t]):
                    sp.wait_ge(probs_set, start[t] + c + 1)
                    sp.dma_start(out_rows[:, t, a:b], probs[:, t, a:b]).then_inc(stored, DMA)
            sp.wait_ge(stored, DMA * chunks)

        @block.gpsimd
        def _(pool):
            pool.memset(ident[:, :], 0.0).then_inc(ident_step, 1)
            pool.wait_ge(ident_step, 1)
            pool.affine_select(out=ident[:, :], in_=ident[:, :], compare_op=ALU.not_equal, fill=1.0,
                               base=0, pattern=[[-1, P]], channel_multiplier=1).then_inc(ident_step, 1)
            pool.wait_ge(index_in, DMA)

            def gather(out, table, t, which, landed):
                pool.indirect_dma_start(
                    out=out, out_offset=None, in_=table,
                    in_offset=bass.IndirectOffsetOnAxis(ap=index[:, t, which:which + 1], axis=0)).then_inc(landed, DMA)

            def users(t):
                gather(emb[t][:, 0:DU], users_emb, t, 0, users_in[t])

            def items(t):
                gather(emb[t][:, DU:D], items_emb, t, 1, items_in[t])

            def whole_rows(t):
                gather(rows[:, t, DU:D + N], item_rows, t, 1, rows_in[t])

            for t in range(0, T, 2):
                users(t)
                items(t)
                whole_rows(t + 1)
                users(t + 1)
                whole_rows(t)
            pool.wait_ge(rows_in[T - 1], DMA)
            pool.wait_ge(bias_copied, len(whole))
            pool.tensor_tensor(scores[:, T - 1, :], scores[:, T - 1, :], bias_wide[:, :], ALU.add).then_inc(biased, 1)

        @block.tensor
        def _(pe):
            def turn(t):
                pe.wait_ge(users_in[t], DMA)
                pe.wait_ge(items_in[t], DMA)
                if t >= 1:
                    pe.wait_ge(h2_set, t)
                pe.transpose(mlp_ps[0:D, 0:P], emb[t], ident[:, :]).then_inc(turned, 1)

            def first(t):
                pe.wait_ge(embT_set, t + 1)
                pe.matmul(mlp_ps[:, 0:P], w1T, embT[:, t % 2, :], start=True, stop=True).then_inc(layer1, 1)

            def second(t):
                pe.wait_ge(h1_set, t + 1)
                pe.matmul(mlp_ps[:, 0:P], w2T, h1[:, t % 2, :], start=True, stop=True).then_inc(layer2, 1)

            def bias(t, c):
                a, b = cols[t][c]
                n = start[t] + c
                if n >= SCORE_BANKS:
                    pe.wait_ge(added, n - SCORE_BANKS + 1)
                return pe.matmul(score_ps[:, n % SCORE_BANKS, 0:b - a], ones[:, :], bias_rows[:, a:b],
                                 start=True, stop=t == 1)

            def score(t, c):
                a, b = cols[t][c]
                n = start[t] + c
                if c == 0:
                    pe.wait_ge(h2_set, t + 1)
                if t == 1:
                    pe.wait_ge(bias_copied, c + 1)
                if t == T - 1:
                    pe.wait_ge(added, n - SCORE_BANKS + 1)
                pe.matmul(score_ps[:, n % SCORE_BANKS, 0:b - a], h2[:, t % 2, :], head_w[:, a:b],
                          start=t == T - 1, stop=True, skip_group_check=t == 1).then_inc(scored, 1)

            def keep_warm(n):
                for _ in range(n):
                    pe.matmul(score_ps[:, SCORE_BANKS - 1, 0:P], ident[:, :], ident[:, :], start=True, stop=True)

            pe.wait_ge(ident_step, 2)
            keep_warm(WARM_UPS)
            pe.wait_ge(weights_in, DMA)
            turn(0)
            keep_warm(1)
            pe.wait_ge(ones_set, 1)
            for k in range(BIAS_PARTS):
                pe.wait_ge(bias_rows_in[k], DMA)
            bias(0, 0)
            bias(0, 1)
            first(0)
            keep_warm(2)
            bias(0, 2)
            bias(1, 0)
            second(0)
            bias(1, 1)
            bias(1, 2).then_inc(bias_made, 1)
            bias(2, 0)
            turn(1)
            pe.wait_ge(head_in, DMA)
            for t in range(T):
                for c in range(len(cols[t])):
                    if start[t] + c >= SCORE_BANKS and t < T - 1:
                        bias(t, c)
                    score(t, c)
                    if c == 0 and t + 1 < T:
                        first(t + 1)
                    if c == 1 and t + 1 < T:
                        second(t + 1)
                if t + 2 < T:
                    turn(t + 2)

        @block.vector
        def _(dve):
            dve.memset(ones[:, :], 1.0).then_inc(ones_set, 1)
            dve.wait_ge(bias_in, DMA)
            rest = bias_raw[:, :]
            for k in range(BIAS_PARTS):
                dve.tensor_copy(bias_part[:, k, :], rest).then_inc(bias_step, 1)
                if k < BIAS_PARTS - 1:
                    dve.wait_ge(bias_step, 2 * k + 1)
                    dve.tensor_tensor(bias_rest[:, k, :], rest, bias_part[:, k, :], ALU.subtract).then_inc(bias_step, 1)
                    dve.wait_ge(bias_step, 2 * k + 2)
                    rest = bias_rest[:, k, :]

            def relu1(t):
                dve.wait_ge(layer1, t + 1)
                dve.tensor_scalar(h1[:, t % 2, :], mlp_ps[:, 0:P], b1, 0.0, ALU.add, ALU.max).then_inc(h1_set, 1)

            def add(t, c):
                a, b = cols[t][c]
                dve.wait_ge(scored, start[t] + c + 1)
                dve.tensor_tensor(scores[:, t, a:b], score_ps[:, (start[t] + c) % SCORE_BANKS, 0:b - a],
                                  scores[:, t, a:b], ALU.add).then_inc(added, 1)

            dve.wait_ge(weights_in, DMA)
            relu1(0)
            for t in range(T):
                if t + 1 < T:
                    relu1(t + 1)
                if t < T - 1:
                    dve.wait_ge(rows_in[t], DMA)
                else:
                    dve.wait_ge(biased, 1)
                for c in range(len(cols[t])):
                    add(t, c)

        @block.scalar
        def _(act):
            act.dma_start(bias_raw[:, :], b_head).then_inc(bias_in, DMA)
            act.dma_start(head_w[:, :], head_h).then_inc(head_in, DMA)
            act.wait_ge(ident_step, 2)
            act.activation(warm[:, :], ident[:, 0:1], ACT.Sigmoid)

            def copy_embT(t):
                act.wait_ge(turned, t + 1)
                act.activation(embT[:, t % 2, :], mlp_ps[0:D, 0:P], ACT.Copy).then_inc(embT_set, 1)

            def relu2(t):
                act.wait_ge(layer2, t + 1)
                act.activation(h2[:, t % 2, :], mlp_ps[:, 0:P], ACT.Relu, bias=b2).then_inc(h2_set, 1)

            def sigmoid(t, c):
                a, b = cols[t][c]
                act.wait_ge(added, start[t] + c + 1)
                act.activation(probs[:, t, a:b], scores[:, t, a:b], ACT.Sigmoid).then_inc(probs_set, 1)

            act.wait_ge(weights_in, DMA)
            copy_embT(0)
            relu2(0)
            copy_embT(1)
            act.wait_ge(bias_made, 1)
            for c, (a, b) in enumerate(whole):
                act.activation(bias_wide[:, a:b], score_ps[:, start[1] + c, 0:b - a], ACT.Copy).then_inc(bias_copied, 1)
            for t in range(T):
                if t + 1 < T:
                    relu2(t + 1)
                if t + 2 < T:
                    copy_embT(t + 2)
                for c in range(len(cols[t])):
                    sigmoid(t, c)


def kernel(r_interactions, L0_rec_users_emb_w, L0_rec_items_emb_w, L0_rec_w1, L0_rec_b1, L0_rec_w2, L0_rec_b2,
           L0_rec_w_head, L0_rec_b_head):
    import numpy as np
    import concourse.bacc as bacc
    from concourse.bass_utils import run_bass_kernel_spmd

    n_items = L0_rec_items_emb_w.shape[0]
    hidden, d_in = L0_rec_w1.shape
    headT = np.ascontiguousarray(np.transpose(L0_rec_w_head))
    item_rows = np.concatenate([L0_rec_items_emb_w, headT[0:n_items]], axis=1)
    mlp_weights = np.zeros((hidden, 2 * hidden + 2), dtype=L0_rec_w1.dtype)
    mlp_weights[0:d_in, 0:hidden] = np.transpose(L0_rec_w1)
    mlp_weights[:, hidden:2 * hidden] = np.transpose(L0_rec_w2)
    mlp_weights[:, 2 * hidden] = L0_rec_b1
    mlp_weights[:, 2 * hidden + 1] = L0_rec_b2
    spread = max(p for p in range(1, 129) if n_items % p == 0)
    arrays = {
        "interactions": np.ascontiguousarray(r_interactions),
        "users_emb": np.ascontiguousarray(L0_rec_users_emb_w),
        "items_emb": np.ascontiguousarray(L0_rec_items_emb_w),
        "item_rows": np.ascontiguousarray(item_rows),
        "mlp_weights": mlp_weights,
        "head_h": np.ascontiguousarray(headT[n_items:]),
        "b_head": np.ascontiguousarray(np.reshape(L0_rec_b_head, (spread, n_items // spread))),
    }
    nc = bacc.Bacc("TRN2", target_bir_lowering=False, num_devices=1)
    args = [nc.dram_tensor(name, a.shape, mybir.dt.from_np(a.dtype), kind="ExternalInput").ap()
            for name, a in arrays.items()]
    out = nc.dram_tensor("item_probs", (r_interactions.shape[0], n_items), F32, kind="ExternalOutput").ap()
    rec_scores_kernel(nc, *args, out)
    ran = run_bass_kernel_spmd(nc, [arrays], core_ids=[0])
    return ran.results[0]["item_probs"]
```
